# Optimizing a Trainium2 kernel written in Bass

```python
import numpy as np
import jax
import jax.numpy as jnp

def _softmax(x, axis=-1):
    return jax.nn.softmax(x, axis=axis)
def _gelu(x):
    return jax.nn.gelu(x, approximate=True)
def _silu(x):
    return jax.nn.silu(x)
def _sigmoid(x):
    return jax.nn.sigmoid(x)
def _layernorm(x, axis=-1, eps=1e-5):
    m = jnp.mean(x, axis=axis, keepdims=True)
    v = jnp.var(x, axis=axis, keepdims=True)
    return (x - m) / jnp.sqrt(v + eps)
def _scatter_add(tgt, idx, src, axis=0):
    return tgt.at[idx].add(src)
def _segment_sum(src, seg, n):
    return jax.ops.segment_sum(src, seg, n)

kernel_name = 'mk_conv_preact_d2_conv_nhwc256_9af07e'

def setup_inputs(seed: int = 0):
    np.random.seed(seed)
    _w = jnp.asarray
    def _rec_inputs():
        import jax
        import jax.numpy as jnp
        _gk = jax.random.key(seed)
        x = -8.268e-05 + 0.9999 * jax.random.normal(jax.random.fold_in(_gk, 1), (16, 112, 112, 256), jnp.float32)
        return x
    x = _rec_inputs()
    def _L0_conv_setup():
        import jax, jax.numpy as jnp
        import numpy as np

        @jax.custom_vjp
        def ste_sign(x):
            return jnp.where(x >= 0, jnp.ones((), x.dtype), -jnp.ones((), x.dtype))

        def _ste_fwd(x):
            return (ste_sign(x), x)

        def _ste_bwd(x, g):
            return (g * (jnp.abs(x) <= 1).astype(g.dtype),)
        ste_sign.defvjp(_ste_fwd, _ste_bwd)
        key = jax.random.key(seed)
        k1, k2 = jax.random.split(key)
        x = jax.random.normal(k1, (16, 112, 112, 256), dtype=jnp.float32)
        kernel = jax.random.normal(k2, (3, 3, 256, 1), dtype=jnp.float32) * 0.1
        return {'x': x, 'kernel': kernel}
    _L0_conv_all = _L0_conv_setup()
    _L0_conv_in = {k: v for k, v in _L0_conv_all.items() if k in ('kernel', )}
    del _L0_conv_all

    def _L1_conv_setup():
        import jax, jax.numpy as jnp
        import numpy as np
        from jax import lax
        B_, H_, W_, C_ = (32, 56, 56, 256)
        RED = 16
        STATE = 16
        EPS = 1e-05

        def _s6(m, A, d_w, d_b, B_w, B_b, C_w, C_b):
            delta = jax.nn.softplus(m @ d_w.T + d_b)
            Bm = m @ B_w.T + B_b
            Cm = m @ C_w.T + C_b
            dA = jnp.exp(delta[..., None] * A)
            dBx = (delta * m)[..., None] * Bm[:, :, None, :]
            a_t = jnp.moveaxis(dA, 1, 0)
            b_t = jnp.moveaxis(dBx, 1, 0)
            c_t = jnp.moveaxis(Cm[:, :, None, :], 1, 0)

            def step(h, abc):
                a, b, c = abc
                h = a * h + b
                y = jnp.sum(h * c, axis=-1)
                return (h, y)
            h0 = jnp.zeros_like(a_t[0])
            _, ys = lax.scan(step, h0, (a_t, b_t, c_t))
            return jnp.moveaxis(ys, 0, 1)
        key = jax.random.key(seed)
        ks = jax.random.split(key, 10)
        x = jax.random.normal(ks[0], (B_, H_, W_, C_), jnp.float32)
        ca_w1 = jax.random.normal(ks[1], (C_ // RED, C_), jnp.float32) * 0.05
        ca_w2 = jax.random.normal(ks[2], (C_, C_ // RED), jnp.float32) * 0.05
        lsa_w = jax.random.normal(ks[3], (7, 7, 2, 1), jnp.float32) * 0.05
        A = -jnp.exp(jax.random.normal(ks[4], (1, STATE), jnp.float32) * 0.5)
        d_w = jax.random.normal(ks[5], (1, 1), jnp.float32) * 0.5
        d_b = jnp.zeros((1,), jnp.float32)
        B_w = jax.random.normal(ks[6], (STATE, 1), jnp.float32) * 0.5
        B_b = jnp.zeros((STATE,), jnp.float32)
        C_w = jax.random.normal(ks[7], (STATE, 1), jnp.float32) * 0.5
        C_b = jnp.zeros((STATE,), jnp.float32)
        bn_gamma = jnp.ones((C_,), jnp.float32)
        bn_beta = jnp.zeros((C_,), jnp.float32)
        return dict(x=x, ca_w1=ca_w1, ca_w2=ca_w2, lsa_w=lsa_w, A=A, d_w=d_w, d_b=d_b, B_w=B_w, B_b=B_b, C_w=C_w, C_b=C_b, bn_gamma=bn_gamma, bn_beta=bn_beta)
    _L1_conv_all = _L1_conv_setup()
    _L1_conv_in = {k: v for k, v in _L1_conv_all.items() if k in ('ca_w1', 'ca_w2', 'lsa_w', 'A', 'd_w', 'd_b', 'B_w', 'B_b', 'C_w', 'C_b', 'bn_gamma', 'bn_beta', )}
    del _L1_conv_all

    return {
        "x": x,
        "L0_conv_kernel": _L0_conv_in["kernel"],
        "L1_conv_ca_w1": _L1_conv_in["ca_w1"],
        "L1_conv_ca_w2": _L1_conv_in["ca_w2"],
        "L1_conv_lsa_w": _L1_conv_in["lsa_w"],
        "L1_conv_A": _L1_conv_in["A"],
        "L1_conv_d_w": _L1_conv_in["d_w"],
        "L1_conv_d_b": _L1_conv_in["d_b"],
        "L1_conv_B_w": _L1_conv_in["B_w"],
        "L1_conv_B_b": _L1_conv_in["B_b"],
        "L1_conv_C_w": _L1_conv_in["C_w"],
        "L1_conv_C_b": _L1_conv_in["C_b"],
        "L1_conv_bn_gamma": _L1_conv_in["bn_gamma"],
        "L1_conv_bn_beta": _L1_conv_in["bn_beta"],
    }

def reference(x, L0_conv_kernel, L1_conv_ca_w1, L1_conv_ca_w2, L1_conv_lsa_w, L1_conv_A, L1_conv_d_w, L1_conv_d_b, L1_conv_B_w, L1_conv_B_b, L1_conv_C_w, L1_conv_C_b, L1_conv_bn_gamma, L1_conv_bn_beta):
    import jax
    import jax.numpy as jnp
    def _L0_conv_ref(x, kernel):
        import jax, jax.numpy as jnp
        import numpy as np

        @jax.custom_vjp
        def ste_sign(x):
            return jnp.where(x >= 0, jnp.ones((), x.dtype), -jnp.ones((), x.dtype))

        def _ste_fwd(x):
            return (ste_sign(x), x)

        def _ste_bwd(x, g):
            return (g * (jnp.abs(x) <= 1).astype(g.dtype),)
        ste_sign.defvjp(_ste_fwd, _ste_bwd)
        xq = ste_sign(x)
        kq = ste_sign(kernel)
        kh, kw, C, mult = kernel.shape
        rhs = kq.reshape(kh, kw, 1, C * mult)
        out = jax.lax.conv_general_dilated(xq, rhs, window_strides=(1, 1), padding='SAME', feature_group_count=C, dimension_numbers=('NHWC', 'HWIO', 'NHWC'))
        return out

    def _L1_conv_ref(x, ca_w1, ca_w2, lsa_w, A, d_w, d_b, B_w, B_b, C_w, C_b, bn_gamma, bn_beta):
        import jax, jax.numpy as jnp
        import numpy as np
        from jax import lax
        B_, H_, W_, C_ = (32, 56, 56, 256)
        RED = 16
        STATE = 16
        EPS = 1e-05

        def _s6(m, A, d_w, d_b, B_w, B_b, C_w, C_b):
            delta = jax.nn.softplus(m @ d_w.T + d_b)
            Bm = m @ B_w.T + B_b
            Cm = m @ C_w.T + C_b
            dA = jnp.exp(delta[..., None] * A)
            dBx = (delta * m)[..., None] * Bm[:, :, None, :]
            a_t = jnp.moveaxis(dA, 1, 0)
            b_t = jnp.moveaxis(dBx, 1, 0)
            c_t = jnp.moveaxis(Cm[:, :, None, :], 1, 0)

            def step(h, abc):
                a, b, c = abc
                h = a * h + b
                y = jnp.sum(h * c, axis=-1)
                return (h, y)
            h0 = jnp.zeros_like(a_t[0])
            _, ys = lax.scan(step, h0, (a_t, b_t, c_t))
            return jnp.moveaxis(ys, 0, 1)
        Bn, H, W, C = x.shape
        avg = jnp.mean(x, axis=(1, 2))
        mx = jnp.max(x, axis=(1, 2))
        fc = lambda v: jax.nn.relu(v @ ca_w1.T) @ ca_w2.T
        ca_gate = jax.nn.sigmoid(fc(avg) + fc(mx))[:, None, None, :]
        xc = x * ca_gate
        m = jnp.mean(xc, axis=-1, keepdims=True).reshape(Bn, H * W, 1)
        y = _s6(m, A, d_w, d_b, B_w, B_b, C_w, C_b).reshape(Bn, H, W, 1)
        ma = xc * jax.nn.sigmoid(y)
        feat = jnp.concatenate([jnp.mean(xc, axis=-1, keepdims=True), jnp.max(xc, axis=-1, keepdims=True)], axis=-1)
        s = lax.conv_general_dilated(feat, lsa_w, (1, 1), 'SAME', dimension_numbers=('NHWC', 'HWIO', 'NHWC'))
        sa = xc * jax.nn.sigmoid(s)
        x2 = ma + sa
        mean = jnp.mean(x2, axis=(0, 1, 2))
        var = jnp.var(x2, axis=(0, 1, 2))
        out = (x2 - mean) * lax.rsqrt(var + EPS) * bn_gamma + bn_beta
        return jax.nn.relu(out)

    def _gn(v, G=32, eps=1e-5):
        B_, H_, W_, C_ = v.shape
        g = v.reshape(B_, H_, W_, G, C_ // G)
        m = jnp.mean(g, axis=(1, 2, 4), keepdims=True)
        s = jnp.var(g, axis=(1, 2, 4), keepdims=True)
        return ((g - m) / jnp.sqrt(s + eps)).reshape(v.shape)

    def _ln_c(v, eps=1e-6):
        m = jnp.mean(v, axis=-1, keepdims=True)
        s = jnp.var(v, axis=-1, keepdims=True)
        return (v - m) / jnp.sqrt(s + eps)

    def _ln_t(v, eps=1e-5):
        m = jnp.mean(v, axis=-1, keepdims=True)
        s = jnp.var(v, axis=-1, keepdims=True)
        return (v - m) / jnp.sqrt(s + eps)

    def _to_tokens(v):
        B_, H_, W_, C_ = v.shape
        return v.reshape(B_, H_ * W_, C_)
    def _from_tokens(t, like):
        return t.reshape(like.shape)

    x = x + _L0_conv_ref(_gn(x), L0_conv_kernel)
    x = x + _L1_conv_ref(_gn(x), L1_conv_ca_w1, L1_conv_ca_w2, L1_conv_lsa_w, L1_conv_A, L1_conv_d_w, L1_conv_d_b, L1_conv_B_w, L1_conv_B_b, L1_conv_C_w, L1_conv_C_b, L1_conv_bn_gamma, L1_conv_bn_beta)
    return x


_drawn_inputs = setup_inputs


def setup_inputs(seed=0):
    import zlib

    import numpy as np

    out = dict(_drawn_inputs(seed))
    spreads = {'L1_conv_B_b': (0.0, 2.0),
     'L1_conv_C_b': (0.0, 2.0),
     'L1_conv_bn_gamma': (1.0, 0.2),
     'L1_conv_bn_beta': (0.0, 0.398)}
    factors = {'L1_conv_ca_w1': 8.0,
     'L1_conv_ca_w2': 8.0,
     'L1_conv_lsa_w': 8.0,
     'L1_conv_A': 64.0,
     'L1_conv_B_w': 200.0,
     'L1_conv_C_w': 199.982}
    for name, (base, spread) in spreads.items():
        noise = np.random.default_rng([zlib.crc32(name.encode()), seed]).standard_normal(out[name].shape)
        drawn = base * np.exp(spread * noise) if base else spread * noise
        out[name] = jnp.asarray(drawn.astype(out[name].dtype))
    for name, factor in factors.items():
        out[name] = (out[name] * factor).astype(out[name].dtype)
    return out
```

```python
import concourse.bass as bass
from concourse import mybir
from contextlib import ExitStack


def binary_conv_then_gated_ssm_block(
    nc: bass.Bass,
    x_d: bass.AP,
    conv_k_d: bass.AP,
    w1_d: bass.AP,
    w2_d: bass.AP,
    lsa_d: bass.AP,
    A_d: bass.AP,
    d_w_d: bass.AP,
    d_b_d: bass.AP,
    B_w_d: bass.AP,
    B_b_d: bass.AP,
    C_w_d: bass.AP,
    C_b_d: bass.AP,
    gamma_d: bass.AP,
    beta_d: bass.AP,
    out_d: bass.AP,
):
    fp32 = mybir.dt.float32
    bf16 = mybir.dt.bfloat16
    fp8 = mybir.dt.float8e4
    u32 = mybir.dt.uint32
    ALU = mybir.AluOpType
    ACT = mybir.ActivationFunctionType
    AX = mybir.AxisListType.X

    P = 128
    NB, H, W, C = x_d.shape
    HW = H * W
    NJ = C // P
    GS = C // 32
    RS = 16
    NS = H // RS
    SP = RS * W
    NT = SP // P
    TG = NT // 2
    TP = TG * P
    RT = TP // W
    HB = RT // 2 * W
    NTILE = NS * NJ * 2
    HP, WP = H + 2, W + 2
    KS, PAD = 7, 3
    NST = A_d.shape[1]
    NRED = w1_d.shape[2]
    GI = min(P // NST, NB)
    NGRP = NB // GI
    NPQ = HW // P
    TC = SP
    EPS = 1e-5
    assert HB * 2 == TP and NT % 2 == 0 and NB % GI == 0

    x1_d = nc.dram_tensor("x1_scratch", (NB, NJ, P, HW), fp32, kind="Internal").ap()
    feat_d = nc.dram_tensor("feat_scratch", (2, NB, HW), fp32, kind="Internal").ap()
    ssm_d = nc.dram_tensor("ssm_scratch", (2, NB, HW), fp32, kind="Internal").ap()
    y_d = nc.dram_tensor("y_scratch", (NB, HW), fp32, kind="Internal").ap()
    gate_d = nc.dram_tensor("gate_scratch", (3, NB, HW), bf16, kind="Internal").ap()

    ctx = ExitStack()
    with ctx:
        def sb(name, shape, dt=fp32):
            return ctx.enter_context(nc.sbuf_tensor(name, shape, dt))

        def pb(name, shape, dt=fp32):
            return ctx.enter_context(nc.psum_tensor(name, shape, dt))

        def sem(name):
            return ctx.enter_context(nc.semaphore(name))

        xt = sb("xt", [P, NJ, HW])
        xin = [sb(f"xin{b}", [P, NT, C]) for b in range(2)]
        xc = [sb(f"xc{b}", [P, NJ, SP]) for b in range(2)]
        signs_raw = sb("signs", [P, (NJ * HP * WP + 3) // 4], u32)
        signs = signs_raw[:, :].bitcast(fp8)[:, 0:NJ * HP * WP].rearrange("p (j h w) -> p j h w", j=NJ, h=HP)
        squares = sb("squares", [P, SP], bf16)
        x1acc = sb("x1acc", [P, NJ, TP])
        taps = sb("taps", [P, NJ, 9, P], bf16)
        kraw = sb("kraw", [P, NJ, 9])
        kval = sb("kval", [P, NJ, 9])
        ident = sb("ident", [P, P])
        groups = sb("groups", [P, P])
        mean_col = sb("mean_col", [P, 1])
        ones3 = sb("ones3", [3, P], bf16)
        w1 = sb("w1", [P, NJ, NRED])
        w2 = sb("w2", [NRED, C])
        xsum_p = sb("xsum_p", [P, NJ, 2 * NS])
        x1max_p = sb("x1max_p", [P, NJ, 2 * NS])
        x1sq_p = sb("x1sq_p", [P, NJ, NS])
        xsum = sb("xsum", [P, NJ])
        mean0 = sb("mean0", [P, NJ])
        nmean0 = sb("nmean0", [P, NJ])
        st = sb("st", [P, 16, NJ])
        fc_in = sb("fc_in", [P, NJ, 2])
        hid2 = sb("hid2", [NRED, 2])
        hid = sb("hid", [NRED, 1])
        cur = sb("cur", [P, 2, NJ])
        par = sb("par", [P, NB, 2 * NJ])
        bnsum = sb("bnsum", [P, NB, 2 * NJ])
        pmean = sb("pmean", [P, NS, NT])
        pmax = sb("pmax", [P, NS, NT])
        gammas = sb("gammas", [P, NJ])
        betas = sb("betas", [P, NJ])

        psum = pb("psum", [P, 8 * 512])
        bank = [psum[:, b * 1024:(b + 1) * 1024] for b in range(4)]
        turn = bank[0:2]
        back = [bank[2][:, 0:512], bank[2][:, 512:1024], bank[3][:, 0:512]]
        small = bank[3][:, 512:1024]
        pix_ps = small[:, 0:NS * NT]
        grp_ps = small[:, 128:128 + NJ]
        st_ps = small[:, 136:136 + 2 * NJ]
        hid_ps = small[0:NRED, 144:146]
        gate_ps = small[:, 152:152 + NJ]

        x_strips = x_d.rearrange("b h w c -> b (h w) c")
        out_strips = out_d.rearrange("b h w c -> b (h w) c")

        def strip(t, j, s):
            return t[:, j, s * SP:(s + 1) * SP]

        def tile_px(j, s, g):
            p0 = s * SP + g * TP
            return xt[:, j, p0:p0 + TP].rearrange("p (b n) -> p b n", b=2)

        def banks(t, n):
            return t.rearrange("p (b n) -> p b n", n=512)[:, :, 0:n]

        class Steps:

            def __init__(self, eng, done, base):
                self.eng, self.done, self.base, self.n = eng, done, base, 0

            def __call__(self, ins):
                ins.then_inc(self.done, 1)
                self.n += 1
                self.eng.wait_ge(self.done, self.base + self.n)

        holds = sem("holds")

        def hold(eng, done, value):
            eng.wait_ge(done, value)
            eng.sem_inc(holds, 1)

        params_in = sem("params_in")
        consts_made = sem("consts_made")
        taps_made = sem("taps_made")
        strip_in = [sem(f"strip_in{b}") for b in range(2)]
        turned = sem("turned")
        evacuated = sem("evacuated")
        xsum_made = sem("xsum_made")
        grp_made = sem("grp_made")
        mean_steps = sem("mean_steps")
        signs_made = sem("signs_made")
        convolved = sem("convolved")
        added = sem("added")
        squared = sem("squared")
        summed = sem("summed")
        stored = sem("stored")
        sums_made = sem("sums_made")
        st_made = sem("st_made")
        st_steps = sem("st_steps")
        var_made = sem("var_made")
        ln_made = sem("ln_made")
        rstd_made = sem("rstd_made")
        fc_in_made = sem("fc_in_made")
        hid_made = sem("hid_made")
        hid_in = sem("hid_in")
        gate_made = sem("gate_made")
        gexp_in = sem("gexp_in")
        gexp_made = sem("gexp_made")
        gated = sem("gated")
        turned_back = sem("turned_back")
        reduced = sem("reduced")
        feats_made = sem("feats_made")
        feats_out = sem("feats_out")
        ST_STEPS = 25
        NSUM = NJ * (2 * NS - 1)

        with nc.Block() as block:
            def load(sp, i, s):
                sp.dma_start(xin[s % 2][:, :, :],
                             x_strips[i, s * SP:(s + 1) * SP, :].rearrange("(p t) c -> p t c", t=NT)
                             ).then_inc(strip_in[s % 2], 16)

            @block.sync
            def _(sp):
                for dst, src in ((kraw, conv_k_d), (w1, w1_d), (w2, w2_d), (gammas, gamma_d), (betas, beta_d)):
                    sp.dma_start(dst[:], src).then_inc(params_in, 16)
                load(sp, 0, 0)
                load(sp, 0, 1)
                for s in range(2, NS):
                    sp.wait_ge(turned, 4 * (s - 1))
                    load(sp, 0, s)

                def image(i, more):
                    if more:
                        sp.wait_ge(turned, i * NTILE + NTILE)
                        load(sp, i + 1, 0)
                        load(sp, i + 1, 1)
                    for s in range(NS):
                        sp.wait_ge(added, i * NTILE + 4 * (s + 1))
                        sp.dma_start(x1_d[i, :, :, s * SP:(s + 1) * SP].rearrange("j c n -> c j n"),
                                     xt[:, :, s * SP:(s + 1) * SP]).then_inc(stored, 16)
                    if more:
                        for s in range(2, NS):
                            sp.wait_ge(turned, i * NTILE + NTILE + 4 * (s - 1))
                            load(sp, i + 1, s)
                    sp.wait_ge(feats_made, i + 1)
                    for k, t in ((0, pmean), (1, pmax)):
                        sp.dma_start(feat_d[k, i, :].rearrange("(s p t) -> p s t", s=NS, p=P),
                                     t[:, :, :]).then_inc(feats_out, 16)

                with sp.Fori(0, NB - 1) as i:
                    image(i, True)
                image(NB - 1, False)
                sp.wait_ge(stored, 16 * NS * NB)
                sp.wait_ge(feats_out, 32 * NB + 1)

            @block.gpsimd
            def _(pool):
                steps = Steps(pool, consts_made, 0)
                steps(nc.gpsimd.memset(ident[:, :], 0.0))
                steps(nc.gpsimd.affine_select(out=ident[:, :], in_=ident[:, :], compare_op=ALU.not_equal, fill=1.0,
                                              base=0, pattern=[[-1, P]], channel_multiplier=1))
                steps(nc.gpsimd.memset(groups[:, :], 1.0))
                view = groups[:, :].rearrange("p (g c) -> p g c", c=GS)
                steps(nc.gpsimd.affine_select(out=view, in_=view, compare_op=ALU.is_ge, fill=0.0,
                                              base=0, pattern=[[-GS, P // GS], [0, GS]], channel_multiplier=1))
                steps(nc.gpsimd.affine_select(out=view, in_=view, compare_op=ALU.is_ge, fill=0.0,
                                              base=GS - 1, pattern=[[GS, P // GS], [0, GS]], channel_multiplier=-1))
                steps(nc.gpsimd.memset(mean_col[:, :], 1.0 / C))
                steps(nc.gpsimd.memset(ones3[:, :], 1.0))
                steps(nc.gpsimd.memset(signs_raw[:, :], 0))

                def image(i):
                    n = 0
                    for s in range(NS):
                        pool.wait_ge(added, i * NTILE + 4 * (s + 1))
                        for j in range(NJ):
                            a = strip(xt, j, s)[:, 0:TP]
                            b = strip(xt, j, s)[:, TP:SP]
                            if s == 0:
                                nc.gpsimd.tensor_tensor(x1acc[:, j, :], a, b, ALU.add).then_inc(summed, 1)
                                n += 1
                                continue
                            for v in (a, b):
                                pool.wait_ge(summed, i * NSUM + n)
                                nc.gpsimd.tensor_tensor(x1acc[:, j, :], x1acc[:, j, :], v, ALU.add).then_inc(summed, 1)
                                n += 1
                    assert n == NSUM

                with pool.Fori(0, NB) as i:
                    image(i)

            def evacuate(act, i, s, reuse):
                if reuse:
                    act.wait_ge(gated, (i - 1) * NS + s + 1)
                for j in range(NJ):
                    for g in range(2):
                        k = 4 * s + 2 * j + g
                        act.wait_ge(turned, i * NTILE + k + 1)
                        dst = strip(xt, j, s).rearrange("c (p t) -> c p t", t=NT)[:, :, g * TG:(g + 1) * TG]
                        src = turn[k % 2][:, 0:TP].rearrange("c (t p) -> c p t", t=TG)
                        nc.scalar.activation(dst, src, ACT.Identity,
                                             accum_out=xsum_p[:, j, 2 * s + g:2 * s + g + 1]).then_inc(evacuated, 1)

            @block.scalar
            def _(act):
                nc.scalar.preload_act_table_set("natural_log_exp_and_others")
                for s in range(NS):
                    evacuate(act, 0, s, False)

                def image(i, more):
                    for s in range(NS):
                        act.wait_ge(added, i * NTILE + 4 * (s + 1))
                        for j in range(NJ):
                            if s or j:
                                act.wait_ge(squared, i * NS * NJ + s * NJ + j)
                            nc.scalar.activation(squares[:, :], strip(xt, j, s), ACT.Square, bias=nmean0[:, j:j + 1],
                                                 accum_out=x1sq_p[:, j, s:s + 1]).then_inc(squared, 1)
                    act.wait_ge(var_made, i + 1)
                    nc.scalar.activation(st[:, 6, :], st[:, 5, :], ACT.Ln).then_inc(ln_made, 1)
                    act.wait_ge(ln_made, i + 1)
                    nc.scalar.activation(st[:, 7, :], st[:, 6, :], ACT.Exp, scale=-0.5).then_inc(rstd_made, 1)
                    act.wait_ge(gexp_in, i + 1)
                    nc.scalar.activation(st[:, 12, :], st[:, 11, :], ACT.Exp).then_inc(gexp_made, 1)
                    if more:
                        act.wait_ge(stored, i * (16 * NS) + 16 * NS)
                        act.wait_ge(summed, i * NSUM + NSUM)
                        for s in range(NS):
                            evacuate(act, i + 1, s, True)

                with act.Fori(0, NB - 1) as i:
                    image(i, True)
                image(NB - 1, False)

            @block.vector
            def _(dve):
                dve.wait_ge(params_in, 80)
                dve.wait_ge(consts_made, 8)
                steps = Steps(dve, taps_made, 0)
                steps(nc.vector.tensor_scalar(kval[:, :, :], kraw[:, :, :], 0.0, 4.0, ALU.is_ge, ALU.mult))
                steps(nc.vector.tensor_scalar(kval[:, :, :], kval[:, :, :], -2.0, None, ALU.add))
                for j in range(NJ):
                    for t in range(9):
                        steps(nc.vector.tensor_scalar(taps[:, j, t, :], ident[:, :], kval[:, j, t:t + 1], None, ALU.mult))

                def mean_of_x(i):
                    steps = Steps(dve, mean_steps, i * 2)
                    dve.wait_ge(evacuated, i * NTILE + NTILE)
                    nc.vector.tensor_reduce(xsum[:, :], xsum_p[:, :, :], AX, ALU.add).then_inc(xsum_made, 1)
                    dve.wait_ge(grp_made, i + 1)
                    steps(nc.vector.tensor_scalar(mean0[:, :], grp_ps, 1.0 / (GS * HW), None, ALU.mult))
                    steps(nc.vector.tensor_scalar(nmean0[:, :], mean0[:, :], -1.0, None, ALU.mult))

                def make_signs(s):
                    for j in range(NJ):
                        last = nc.vector.tensor_scalar(
                            signs[:, j, 1 + s * RS:1 + (s + 1) * RS, 1:1 + W],
                            strip(xt, j, s).rearrange("p (h w) -> p h w", w=W),
                            mean0[:, j:j + 1], 0.5, ALU.is_ge, ALU.subtract, saturate=False)
                    last.then_inc(signs_made, 1)

                def statistics(i):
                    steps = Steps(dve, st_steps, i * ST_STEPS)
                    m1, e2, d, var, rs, t = (st[:, k, :] for k in (2, 3, 4, 5, 7, 8))
                    dve.wait_ge(added, i * NTILE + NTILE)
                    steps(nc.vector.tensor_reduce(st[:, 9, :], x1max_p[:, :, :], AX, ALU.max))
                    dve.wait_ge(squared, i * (NS * NJ) + NS * NJ)
                    steps(nc.vector.tensor_reduce(st[:, 1, :], x1sq_p[:, :, :], AX, ALU.add))
                    dve.wait_ge(summed, i * NSUM + NSUM)
                    steps(nc.vector.tensor_reduce(st[:, 0, :], x1acc[:, :, :], AX, ALU.add))
                    dve.sem_inc(sums_made, 1)
                    dve.wait_ge(st_made, i + 1)
                    steps(nc.vector.tensor_scalar(m1, st_ps[:, 0:NJ], 1.0 / (GS * HW), None, ALU.mult))
                    steps(nc.vector.tensor_scalar(e2, st_ps[:, NJ:2 * NJ], 1.0 / (GS * HW), None, ALU.mult))
                    steps(nc.vector.tensor_tensor(d, m1, mean0[:, :], ALU.subtract))
                    steps(nc.vector.tensor_tensor(d, d, d, ALU.mult))
                    steps(nc.vector.tensor_tensor(var, e2, d, ALU.subtract))
                    steps(nc.vector.tensor_scalar(var, var, 0.0, EPS, ALU.max, ALU.add))
                    dve.sem_inc(var_made, 1)
                    dve.wait_ge(rstd_made, i + 1)
                    steps(nc.vector.tensor_tensor(t, var, rs, ALU.mult))
                    steps(nc.vector.tensor_tensor(t, t, rs, ALU.mult))
                    steps(nc.vector.tensor_scalar(t, t, -0.5, 1.5, ALU.mult, ALU.add))
                    steps(nc.vector.tensor_tensor(rs, rs, t, ALU.mult))
                    steps(nc.vector.scalar_tensor_tensor(t, st[:, 0, :], 1.0 / HW, m1, ALU.mult, ALU.subtract))
                    steps(nc.vector.tensor_tensor(fc_in[:, :, 0], t, rs, ALU.mult))
                    steps(nc.vector.tensor_tensor(st[:, 10, :], st[:, 9, :], m1, ALU.subtract))
                    steps(nc.vector.tensor_tensor(fc_in[:, :, 1], st[:, 10, :], rs, ALU.mult))
                    dve.sem_inc(fc_in_made, 1)
                    dve.wait_ge(hid_made, i + 1)
                    steps(nc.vector.tensor_scalar(hid2[:, :], hid_ps, 0.0, None, ALU.max))
                    steps(nc.vector.tensor_tensor(hid[:, :], hid2[:, 0:1], hid2[:, 1:2], ALU.add))
                    dve.sem_inc(hid_in, 1)
                    dve.wait_ge(gate_made, i + 1)
                    steps(nc.vector.tensor_scalar(st[:, 11, :], gate_ps, -1.0, 80.0, ALU.mult, ALU.min))
                    dve.sem_inc(gexp_in, 1)
                    dve.wait_ge(gexp_made, i + 1)
                    steps(nc.vector.tensor_scalar(st[:, 13, :], st[:, 12, :], 1.0, None, ALU.add))
                    steps(nc.vector.reciprocal(st[:, 14, :], st[:, 13, :]))
                    steps(nc.vector.tensor_tensor(cur[:, 1, :], rs, st[:, 14, :], ALU.mult))
                    steps(nc.vector.tensor_scalar(cur[:, 0, :], m1, -1.0, None, ALU.mult))
                    steps(nc.vector.tensor_copy(par[:, bass.ds(i, 1), :],
                                                cur[:, :, :].rearrange("p (o a) j -> p o (a j)", o=1)))
                    assert steps.n == ST_STEPS, steps.n

                def make_gated(s):
                    for j in range(NJ):
                        last = nc.vector.tensor_scalar(xc[s % 2][:, j, :], strip(xt, j, s), cur[:, 0, j:j + 1],
                                                       cur[:, 1, j:j + 1], ALU.add, ALU.mult)
                    last.then_inc(gated, 1)

                mean_of_x(0)

                def image(i, more):
                    make_signs(0)
                    for s in range(NS):
                        if s + 1 < NS:
                            make_signs(s + 1)
                        for j in range(NJ):
                            for g in range(2):
                                k = 4 * s + 2 * j + g
                                hold(dve, convolved, i * NTILE + k + 1)
                                nc.vector.tensor_tensor_reduce(
                                    out=tile_px(j, s, g), in0=banks(turn[k % 2], HB), in1=tile_px(j, s, g),
                                    scale=1.0, scalar=-3.0e38, op0=ALU.add, op1=ALU.max,
                                    accum_out=x1max_p[:, j, 2 * s + g:2 * s + g + 1]).then_inc(added, 1)
                    statistics(i)
                    make_gated(0)
                    make_gated(1)
                    dve.wait_ge(feats_out, i * 32 + 1)
                    for s in range(NS):
                        for k in range(TG):
                            n = TG * s + k
                            dve.wait_ge(turned_back, i * (TG * NS) + n + 1)
                            nc.vector.tensor_reduce(pmax[:, s, 2 * k:2 * k + 2],
                                                    back[n % 3].rearrange("p (t c) -> p t c", c=C),
                                                    AX, ALU.max).then_inc(reduced, 1)
                        if s + 2 < NS:
                            make_gated(s + 2)
                    nc.vector.tensor_copy(pmean[:, :, :].rearrange("p s t -> p (s t)"), pix_ps).then_inc(feats_made, 1)
                    if more:
                        mean_of_x(i + 1)

                dve.sem_inc(feats_out, 1)
                with dve.Fori(0, NB - 1) as i:
                    image(i, True)
                image(NB - 1, False)

            @block.tensor
            def _(pe):
                pe.wait_ge(consts_made, 8)

                def turn_strip(i, s):
                    b, per = s % 2, 16 * ((NS + 1 - s % 2) // 2)
                    pe.wait_ge(strip_in[b], i * per + 16 * (s // 2 + 1))
                    for j in range(NJ):
                        for g in range(2):
                            k = 4 * s + 2 * j + g
                            if k >= 2:
                                pe.wait_ge(evacuated, i * NTILE + k - 1)
                            for t in range(TG):
                                last = nc.tensor.transpose(turn[k % 2][:, t * P:(t + 1) * P],
                                                           xin[b][:, g * TG + t, j * P:(j + 1) * P], ident[:, :])
                            last.then_inc(turned, 1)

                def group_sums(i):
                    pe.wait_ge(xsum_made, i + 1)
                    nc.tensor.matmul(grp_ps, groups[:, :], xsum[:, :], start=True, stop=True).then_inc(grp_made, 1)

                for s in range(NS):
                    turn_strip(0, s)
                group_sums(0)
                pe.wait_ge(taps_made, 2 + 9 * NJ)

                def image(i, more):
                    for s in range(NS):
                        hold(pe, signs_made, i * NS + min(s + 2, NS))
                        for j in range(NJ):
                            for g in range(2):
                                k = 4 * s + 2 * j + g
                                if k >= 2:
                                    hold(pe, added, i * NTILE + k - 1)
                                for t in range(9):
                                    dh, dw = divmod(t, 3)
                                    for b in range(2):
                                        r = s * RS + g * RT + b * (RT // 2) + dh
                                        last = nc.tensor.matmul(
                                            turn[k % 2][:, b * 512:b * 512 + HB], taps[:, j, t, :],
                                            signs[:, j, r:r + RT // 2, dw:dw + W], start=t == 0, stop=t == 8)
                                last.then_inc(convolved, 1)
                    pe.wait_ge(sums_made, i + 1)
                    nc.tensor.matmul(st_ps, groups[:, :], st[:, 0:2, :].rearrange("p a j -> p (a j)"),
                                     start=True, stop=True).then_inc(st_made, 1)
                    pe.wait_ge(fc_in_made, i + 1)
                    for j in range(NJ):
                        last = nc.tensor.matmul(hid_ps, w1[:, j, :], fc_in[:, j, :], start=j == 0, stop=j == NJ - 1)
                    last.then_inc(hid_made, 1)
                    pe.wait_ge(hid_in, i + 1)
                    for j in range(NJ):
                        last = nc.tensor.matmul(gate_ps[:, j:j + 1], w2[:, j * P:(j + 1) * P], hid[:, :],
                                                start=True, stop=True)
                    last.then_inc(gate_made, 1)
                    for s in range(NS):
                        pe.wait_ge(gated, i * NS + s + 1)
                        for k in range(TG):
                            n = TG * s + k
                            if n >= 3:
                                pe.wait_ge(reduced, i * (TG * NS) + n - 2)
                            for u in range(2):
                                t = 2 * k + u
                                blocks = [xc[s % 2][:, j, :].rearrange("c (p t) -> c t p", t=NT)[:, t, :]
                                          for j in range(NJ)]
                                for j in range(NJ):
                                    nc.tensor.matmul(pix_ps[:, NT * s + t:NT * s + t + 1], blocks[j], mean_col[:, :],
                                                     start=j == 0, stop=j == NJ - 1)
                                for j in range(NJ):
                                    last = nc.tensor.transpose(back[n % 3][:, u * C + j * P:u * C + (j + 1) * P],
                                                               blocks[j], ident[:, :])
                            last.then_inc(turned_back, 1)
                        if more:
                            turn_strip(i + 1, s)
                    if more:
                        group_sums(i + 1)

                with pe.Fori(0, NB - 1) as i:
                    image(i, True)
                image(NB - 1, False)

        flat = xt[:, :, :].rearrange("p j n -> p (j n)")

        def piece(k, n=SP, parts=P):
            return flat[0:parts, k * SP:k * SP + n]

        NQ = NB * NPQ
        assert NQ <= SP and NB * W <= SP
        pix = [piece(k, NQ) for k in range(5)]
        scan_in = [[piece(3 * b + k, TC) for k in range(3)] for b in range(2)]
        decay, bm, hs, cm = (piece(k, TC) for k in (6, 7, 8, 9))
        yrow = [piece(10, TC, GI), piece(11, TC, GI)]
        carry = sb("carry", [P, 1])
        scol = sb("scol", [P, 6])
        dcol = sb("dcol", [P, 2])
        states = sb("states", [P, GI])
        lsa = sb("lsa", [H, KS * KS * 2])
        shifts = sb("shifts", [H, H + KS - 1])
        bands = xin[0][0:H, 0:7, :].rearrange("p t c -> p (t c)")[:, 0:KS * 2 * H].rearrange(
            "p (d k h) -> p d k h", d=KS, k=2)
        WQ = W + KS - 1
        fpad = [xc[k][0:H, :, :].rearrange("p j n -> p (j n)")[:, 0:NB * WQ].rearrange("p (b w) -> p b w", w=WQ)
                for k in range(2)]
        s_out = piece(12, NB * W, H)
        y_in = piece(13, NB * W, H)
        split = xin[1][0:H, :, :].rearrange("p t c -> p (t c)").bitcast(bf16)[:, 0:3 * NB * W].rearrange(
            "p (k n) -> p k n", k=3)

        p2_params = sem("p2_params")
        p2_consts = sem("p2_consts")
        feat_in = sem("feat_in")
        pads_made = sem("pads_made")
        lsa_in = sem("lsa_in")
        conv_in = sem("conv_in")
        delta_steps = sem("delta_steps")
        delta_act = sem("delta_act")
        delta_go = sem("delta_go")
        delta_out = sem("delta_out")
        chunk_in = [sem(f"chunk_in{b}") for b in range(2)]
        decay_made = sem("decay_made")
        cm_made = sem("cm_made")
        bm_made = sem("bm_made")
        scan_steps = sem("scan_steps")
        hc_made = sem("hc_made")
        y_made = sem("y_made")
        y_evac = sem("y_evac")
        y_out = [sem(f"y_out{b}") for b in range(2)]
        y_back = sem("y_back")
        band_steps = sem("band_steps")
        s_made = sem("s_made")
        s_sig = sem("s_sig")
        split_steps = sem("split_steps")
        split_made = sem("split_made")
        gates_out = sem("gates_out")
        NCH = HW // TC
        s_bank = bank[2:4]
        y_ps = banks(psum[0:GI, 0:4 * 512], TC // 4)
        IB = max(1, 512 // W)
        NSB = -(-NB // IB)

        with nc.Block() as block:
            def store_y(sp, n):
                g, c = divmod(n, NCH)
                sp.wait_ge(y_evac, n + 1)
                sp.dma_start(y_d[g * GI:(g + 1) * GI, c * TC:(c + 1) * TC], yrow[n % 2]).then_inc(y_out[n % 2], 16)

            def evac_y(act, n):
                act.wait_ge(y_made, n + 1)
                if n >= 2:
                    act.wait_ge(y_out[n % 2], 16 * (n // 2))
                nc.scalar.activation(yrow[n % 2].rearrange("p (b n) -> p b n", b=4),
                                     y_ps, ACT.Identity).then_inc(y_evac, 1)

            @block.sync
            def _(sp):
                for src, col in ((A_d[0, :], 0), (B_w_d[:, 0], 1), (B_b_d, 2), (C_w_d[:, 0], 3), (C_b_d, 4)):
                    for i in range(GI):
                        sp.dma_start(scol[i * NST:(i + 1) * NST, col:col + 1],
                                     src.rearrange("(n o) -> n o", o=1)).then_inc(p2_params, 16)
                for src, col in ((d_w_d[0, :], 0), (d_b_d, 1)):
                    sp.dma_start(dcol[:, col:col + 1],
                                 src.rearrange("(n o) -> n o", o=1).broadcast_to([P, 1])).then_inc(p2_params, 16)
                sp.dma_start(lsa[:, :], lsa_d.broadcast_to([H, KS * KS * 2])).then_inc(lsa_in, 16)
                sp.dma_start(pix[0].rearrange("p (b q) -> p b q", b=NB),
                             feat_d[0, :, :].rearrange("b (p q) -> p b q", p=P)).then_inc(feat_in, 16)
                sp.wait_ge(pads_made, 2)
                for k in range(2):
                    for b in range(NB):
                        sp.dma_start(fpad[k][:, b, PAD:PAD + W],
                                     feat_d[k, b, :].rearrange("(h w) -> h w", w=W)).then_inc(conv_in, 16)
                sp.wait_ge(delta_go, 1)
                for k, t in ((0, pix[4]), (1, pix[1])):
                    sp.dma_start(ssm_d[k, :, :].rearrange("b (p q) -> p b q", p=P),
                                 t.rearrange("p (b q) -> p b q", b=NB)).then_inc(delta_out, 16)
                sp.wait_ge(delta_out, 32)
                for g in range(NGRP):
                    for c in range(NCH):
                        n = g * NCH + c
                        b = n % 2
                        if n >= 2:
                            sp.wait_ge(hc_made, n - 1)
                        for k, src in ((0, feat_d[0]), (1, ssm_d[0]), (2, ssm_d[1])):
                            for i in range(GI):
                                sp.dma_start(scan_in[b][k][i * NST:(i + 1) * NST, :],
                                             src[g * GI + i:g * GI + i + 1, c * TC:(c + 1) * TC].broadcast_to([NST, TC])
                                             ).then_inc(chunk_in[b], 16)
                        if n >= 1:
                            store_y(sp, n - 1)
                store_y(sp, NGRP * NCH - 1)
                for b in range(2):
                    sp.wait_ge(y_out[b], 16 * ((NGRP * NCH + 1 - b) // 2))
                for b in range(NB):
                    sp.dma_start(y_in[:, b * W:(b + 1) * W],
                                 y_d[b, :].rearrange("(h w) -> h w", w=W)).then_inc(y_back, 16)
                sp.wait_ge(split_made, 1)
                for k in range(3):
                    sp.dma_start(gate_d[k, :, :].rearrange("b (h w) -> h b w", w=W),
                                 split[:, k, :].rearrange("h (b w) -> h b w", w=W)).then_inc(gates_out, 16)
                sp.wait_ge(gates_out, 48)

            @block.gpsimd
            def _(pool):
                steps = Steps(pool, p2_consts, 0)
                steps(nc.gpsimd.memset(states[:, :], 1.0))
                steps(nc.gpsimd.affine_select(out=states[:, :], in_=states[:, :], compare_op=ALU.is_ge, fill=0.0,
                                              base=0, pattern=[[-NST, GI]], channel_multiplier=1))
                steps(nc.gpsimd.affine_select(out=states[:, :], in_=states[:, :], compare_op=ALU.is_ge, fill=0.0,
                                              base=NST - 1, pattern=[[NST, GI]], channel_multiplier=-1))
                steps(nc.gpsimd.memset(shifts[:, :], 0.0))
                steps(nc.gpsimd.affine_select(out=shifts[:, :], in_=shifts[:, :], compare_op=ALU.not_equal, fill=1.0,
                                              base=PAD, pattern=[[-1, H + KS - 1]], channel_multiplier=1))
                pool.wait_ge(p2_params, 16 * (5 * GI + 2))
                for n in range(NGRP * NCH):
                    b = n % 2
                    pool.wait_ge(chunk_in[b], 48 * GI * (n // 2 + 1))
                    if n >= 1:
                        pool.wait_ge(hc_made, n)
                    R = GI * NST
                    nc.gpsimd.tensor_scalar(bm[0:R], scan_in[b][0][0:R], scol[0:R, 1:2], scol[0:R, 2:3],
                                            ALU.mult, ALU.add).then_inc(bm_made, 1)
                    nc.gpsimd.tensor_scalar(cm[0:R], scan_in[b][0][0:R], scol[0:R, 3:4], scol[0:R, 4:5],
                                            ALU.mult, ALU.add).then_inc(cm_made, 1)

            @block.scalar
            def _(act):
                act.wait_ge(delta_steps, 3)
                nc.scalar.activation(pix[3], pix[2], ACT.Exp, scale=-1.0).then_inc(delta_act, 1)
                act.wait_ge(delta_steps, 4)
                nc.scalar.activation(pix[2], pix[4], ACT.Ln).then_inc(delta_act, 1)
                R = GI * NST
                act.wait_ge(p2_params, 16 * (5 * GI + 2))
                for n in range(NGRP * NCH):
                    b = n % 2
                    act.wait_ge(chunk_in[b], 48 * GI * (n // 2 + 1))
                    if n >= 1:
                        act.wait_ge(hc_made, n)
                    nc.scalar.activation(decay[0:R], scan_in[b][1][0:R], ACT.Exp,
                                         scale=scol[0:R, 0:1]).then_inc(decay_made, 1)
                    if n >= 1:
                        evac_y(act, n - 1)
                evac_y(act, NGRP * NCH - 1)
                act.wait_ge(s_made, 1)
                for b in range(NSB):
                    k = min(IB, NB - b * IB)
                    act_last = nc.scalar.activation(s_out[:, b * IB * W:(b * IB + k) * W],
                                                    s_bank[b // 2][0:H, (b % 2) * 512:(b % 2) * 512 + k * W],
                                                    ACT.Sigmoid)
                act_last.then_inc(s_sig, 1)
                act.wait_ge(y_back, 16 * NB)
                nc.scalar.activation(y_in, y_in, ACT.Sigmoid).then_inc(s_sig, 1)

            @block.vector
            def _(dve):
                steps = Steps(dve, pads_made, 0)
                for k in range(2):
                    steps(nc.vector.memset(fpad[k], 0.0))
                dve.wait_ge(feat_in, 16)
                dve.wait_ge(p2_params, 16 * (5 * GI + 2))
                steps = Steps(dve, delta_steps, 0)
                z, az, e, u = pix[1], pix[2], pix[3], pix[4]
                steps(nc.vector.tensor_scalar(z, pix[0], dcol[:, 0:1], dcol[:, 1:2], ALU.mult, ALU.add))
                steps(nc.vector.tensor_scalar(az, z, -1.0, None, ALU.mult))
                steps(nc.vector.tensor_tensor(az, az, z, ALU.max))
                dve.wait_ge(delta_act, 1)
                steps(nc.vector.tensor_scalar(u, e, 1.0, None, ALU.add))
                dve.wait_ge(delta_act, 2)
                steps(nc.vector.tensor_scalar(u, u, -1.0, 2.0 ** -24, ALU.add, ALU.max))
                steps(nc.vector.reciprocal(u, u))
                steps(nc.vector.tensor_tensor(u, u, e, ALU.mult))
                steps(nc.vector.tensor_tensor(u, u, az, ALU.mult))
                steps(nc.vector.scalar_tensor_tensor(u, z, 0.0, u, ALU.max, ALU.add))
                steps(nc.vector.tensor_tensor(z, u, pix[0], ALU.mult))
                dve.sem_inc(delta_go, 1)
                dve.wait_ge(lsa_in, 16)
                dve.wait_ge(p2_consts, 5)
                steps = Steps(dve, band_steps, 0)
                for dw in range(KS):
                    for k in range(2):
                        for dh in range(KS):
                            at = (dh * KS + dw) * 2 + k
                            if dh == 0:
                                steps(nc.vector.tensor_scalar(bands[:, dw, k, :], shifts[:, 0:H], lsa[:, at:at + 1],
                                                              None, ALU.mult))
                            else:
                                steps(nc.vector.scalar_tensor_tensor(
                                    bands[:, dw, k, :], shifts[:, dh:dh + H], lsa[:, at:at + 1], bands[:, dw, k, :],
                                    ALU.mult, ALU.add))
                R = GI * NST
                dx = bm[0:R]
                steps = Steps(dve, scan_steps, 0)
                for n in range(NGRP * NCH):
                    b = n % 2
                    dve.wait_ge(chunk_in[b], 48 * GI * (n // 2 + 1))
                    dve.wait_ge(bm_made, n + 1)
                    steps(nc.vector.tensor_tensor(dx, bm[0:R], scan_in[b][2][0:R], ALU.mult))
                    dve.wait_ge(decay_made, n + 1)
                    if n >= 1:
                        dve.wait_ge(y_made, n)
                    steps(nc.vector.tensor_tensor_scan(hs[0:R], decay[0:R], dx,
                                                       0.0 if n % NCH == 0 else carry[0:R, :], ALU.mult, ALU.add))
                    steps(nc.vector.tensor_copy(carry[0:R, :], hs[0:R, TC - 1:TC]))
                    dve.wait_ge(cm_made, n + 1)
                    nc.vector.tensor_tensor(hs[0:R], hs[0:R], cm[0:R], ALU.mult).then_inc(hc_made, 1)
                steps = Steps(dve, split_steps, 0)
                dve.wait_ge(s_sig, 2)
                steps(nc.vector.tensor_tensor(s_out, s_out, y_in, ALU.add))
                steps(nc.vector.tensor_copy(split[:, 0, :], s_out))
                steps(nc.vector.tensor_tensor(s_out, s_out, split[:, 0, :], ALU.subtract))
                steps(nc.vector.tensor_copy(split[:, 1, :], s_out))
                steps(nc.vector.tensor_tensor(s_out, s_out, split[:, 1, :], ALU.subtract))
                nc.vector.tensor_copy(split[:, 2, :], s_out).then_inc(split_made, 1)

            @block.tensor
            def _(pe):
                pe.wait_ge(band_steps, KS * 2 * KS)
                pe.wait_ge(conv_in, 16 * 2 * NB)
                for b in range(NSB):
                    k = min(IB, NB - b * IB)
                    out = s_bank[b // 2][0:H, (b % 2) * 512:(b % 2) * 512 + k * W]
                    for dw in range(KS):
                        for f in range(2):
                            last = nc.tensor.matmul(out, bands[:, dw, f, :], fpad[f][:, b * IB:b * IB + k, dw:dw + W],
                                                    start=dw == 0 and f == 0, stop=dw == KS - 1 and f == 1)
                last.then_inc(s_made, 1)
                R = GI * NST
                for n in range(NGRP * NCH):
                    pe.wait_ge(hc_made, n + 1)
                    if n >= 1:
                        pe.wait_ge(y_evac, n)
                    for q in range(4):
                        last = nc.tensor.matmul(y_ps[:, q, :], states[0:R, :],
                                                hs[0:R, q * (TC // 4):(q + 1) * (TC // 4)], start=True, stop=True)
                    last.then_inc(y_made, 1)

        NN = 2 * NS
        NIT = NB // 2
        assert NB % 2 == 0
        slots = [flat[:, s * NJ * SP:(s + 1) * NJ * SP].rearrange("p (j n) -> p j n", j=NJ) for s in range(NS)]
        gate_rows = signs_raw[0:3, :].bitcast(bf16)[:, 0:NS * SP]
        BW = SP // 4

        def load_slot(sp, arrived, i, s):
            sp.dma_start(slots[s], x1_d[i, :, :, s * SP:(s + 1) * SP].rearrange("j c n -> c j n")
                         ).then_inc(arrived[s], 16)
            sp.dma_start(gate_rows[:, s * SP:(s + 1) * SP], gate_d[:, i, s * SP:(s + 1) * SP]
                         ).then_inc(arrived[s], 16)

        def broadcast_gate(dst, s):
            for b in range(4):
                last = nc.tensor.matmul(dst[:, b, :], ones3[:, :],
                                        gate_rows[:, s * SP + b * BW:s * SP + (b + 1) * BW], start=True, stop=True)
            return last

        def fours(t):
            return t.rearrange("p (b n) -> p b n", b=4)

        curs = sb("curs", [P, 2, 2 * NJ])
        g1_p = sb("g1_p", [P, NJ, NS])
        g2_p = sb("g2_p", [P, NJ, NS])
        wsum = sb("wsum", [P, NB, 2 * NJ])
        bn = sb("bn", [P, 12, NJ])

        arrived3 = [sem(f"arrived3_{s}") for s in range(NS)]
        spread3 = sem("spread3")
        u_made3 = sem("u_made3")
        cur_made3 = sem("cur_made3")
        squared3 = sem("squared3")
        reduced3 = sem("reduced3")
        bn_steps = sem("bn_steps")
        bn_var = sem("bn_var")
        bn_ln = sem("bn_ln")
        bn_exp = sem("bn_exp")
        gate_ps3 = [banks(psum[:, b * 2048:(b + 1) * 2048], BW) for b in range(2)]
        U3, Q3 = 3, 4

        with nc.Block() as block:
            @block.sync
            def _(sp):
                for s in range(NS):
                    load_slot(sp, arrived3, 0, s)

                def step(it, more):
                    for n in range(NN):
                        if n < NS or more:
                            sp.wait_ge(u_made3, it * (2 * NN) + 2 * (n + 1) + U3)
                            load_slot(sp, arrived3, it * 2 + n // NS + 1, n % NS)

                if NIT > 1:
                    with sp.Fori(0, NIT - 1) as it:
                        step(it, True)
                step(NIT - 1, False)

            @block.tensor
            def _(pe):
                with pe.Fori(0, NIT) as it:
                    for n in range(NN):
                        pe.wait_ge(arrived3[n % NS], it * 64 + 32 * (n // NS + 1))
                        pe.wait_ge(u_made3, it * (2 * NN) + 2 * (n - 1) + U3)
                        broadcast_gate(gate_ps3[n % 2], n % NS).then_inc(spread3, 1)

            @block.scalar
            def _(act):
                act.sem_inc(squared3, Q3)
                with act.Fori(0, NIT) as it:
                    for n in range(NN):
                        for j in range(NJ):
                            act.wait_ge(u_made3, it * (2 * NN) + 2 * n + j + 1 + U3)
                            u = xc[n % 2][:, j, :]
                            nc.scalar.activation(u, u, ACT.Square,
                                                 accum_out=g2_p[:, j, n % NS:n % NS + 1]).then_inc(squared3, 1)
                act.wait_ge(bn_var, 1)
                nc.scalar.activation(bn[:, 4, :], bn[:, 3, :], ACT.Ln).then_inc(bn_ln, 1)
                act.wait_ge(bn_ln, 1)
                nc.scalar.activation(bn[:, 5, :], bn[:, 4, :], ACT.Exp, scale=-0.5).then_inc(bn_exp, 1)

            @block.vector
            def _(dve):
                dve.sem_inc(u_made3, U3)
                with dve.Fori(0, NIT) as it:
                    for n in range(NN):
                        h, s = divmod(n, NS)
                        if s == 0:
                            nc.vector.tensor_copy(curs[:, h:h + 1, :], par[:, bass.ds(it * 2 + h, 1), :]
                                                  ).then_inc(cur_made3, 1)
                            dve.wait_ge(cur_made3, it * 2 + h + 1)
                        dve.wait_ge(spread3, it * NN + n + 1)
                        for j in range(NJ):
                            dve.wait_ge(squared3, it * (2 * NN) + 2 * (n - 2) + j + 1 + Q3)
                            nc.vector.scalar_tensor_tensor(
                                fours(xc[n % 2][:, j, :]), fours(slots[s][:, j, :]), curs[:, h, j:j + 1],
                                gate_ps3[n % 2], ALU.add, ALU.mult,
                                accum_out=g1_p[:, j, s:s + 1]).then_inc(u_made3, 1)
                        if s == NS - 1:
                            dve.wait_ge(squared3, it * (2 * NN) + 2 * (n + 1) + Q3)
                            dve.wait_ge(u_made3, it * (2 * NN) + 2 * (n + 1) + U3)
                            for k, t in ((0, g1_p), (1, g2_p)):
                                nc.vector.tensor_reduce(bnsum[:, bass.ds(it * 2 + h, 1), k * NJ:(k + 1) * NJ],
                                                        t[:, :, :].rearrange("p (o j) s -> p o j s", o=1),
                                                        AX, ALU.add).then_inc(reduced3, 1)
                steps = Steps(dve, bn_steps, 0)
                dve.wait_ge(reduced3, 2 * NB)
                count = 1.0 / (NB * HW)
                scales = par[:, :, NJ:2 * NJ]
                steps(nc.vector.tensor_tensor(wsum[:, :, 0:NJ], bnsum[:, :, 0:NJ], scales, ALU.mult))
                steps(nc.vector.tensor_tensor(wsum[:, :, NJ:2 * NJ], bnsum[:, :, NJ:2 * NJ], scales, ALU.mult))
                steps(nc.vector.tensor_tensor(wsum[:, :, NJ:2 * NJ], wsum[:, :, NJ:2 * NJ], scales, ALU.mult))
                steps(nc.vector.tensor_reduce(bn[:, 0:2, :].rearrange("p a j -> p (a j)"),
                                              wsum[:, :, :].rearrange("p b k -> p k b"), AX, ALU.add))
                mean, e2, t, var, rs = (bn[:, k, :] for k in (0, 1, 2, 3, 5))
                steps(nc.vector.tensor_scalar(bn[:, 0:2, :], bn[:, 0:2, :], count, None, ALU.mult))
                steps(nc.vector.tensor_tensor(t, mean, mean, ALU.mult))
                steps(nc.vector.tensor_tensor(var, e2, t, ALU.subtract))
                steps(nc.vector.tensor_scalar(var, var, 0.0, EPS, ALU.max, ALU.add))
                dve.sem_inc(bn_var, 1)
                dve.wait_ge(bn_exp, 1)
                steps(nc.vector.tensor_tensor(t, var, rs, ALU.mult))
                steps(nc.vector.tensor_tensor(t, t, rs, ALU.mult))
                steps(nc.vector.tensor_scalar(t, t, -0.5, 1.5, ALU.mult, ALU.add))
                steps(nc.vector.tensor_tensor(rs, rs, t, ALU.mult))
                scale, shift = bn[:, 6, :], bn[:, 7, :]
                steps(nc.vector.tensor_tensor(scale, rs, gammas[:, :], ALU.mult))
                steps(nc.vector.tensor_tensor(t, mean, scale, ALU.mult))
                steps(nc.vector.tensor_tensor(shift, betas[:, :], t, ALU.subtract))
                for j in range(NJ):
                    steps(nc.vector.tensor_scalar(par[:, :, NJ + j], par[:, :, NJ + j], scale[:, j:j + 1],
                                                  None, ALU.mult))

        arrived4 = [sem(f"arrived4_{s}") for s in range(NS)]
        spread4 = sem("spread4")
        cur_made4 = sem("cur_made4")
        u_made4 = sem("u_made4")
        relu_made = sem("relu_made")
        x2_made = sem("x2_made")
        turned4 = sem("turned4")
        staged = sem("staged")
        written = [sem(f"written{b}") for b in range(2)]
        gate_ps4 = banks(psum[:, 0:2048], BW)
        out_ps = [psum[:, (4 + b) * 512:(5 + b) * 512] for b in range(4)]
        T4, E4, W4 = TG + 1, 3, 1

        with nc.Block() as block:
            @block.sync
            def _(sp):
                for s in range(NS):
                    load_slot(sp, arrived4, 0, s)

                def step(it, more):
                    for n in range(NN):
                        i, s = it * 2 + n // NS, n % NS
                        sp.wait_ge(staged, it * (NN * TG) + (n + 1) * TG + E4)
                        sp.dma_start(out_strips[i, s * SP:(s + 1) * SP, :].rearrange("(p t) c -> p t c", t=NT),
                                     xin[n % 2][:, :, :]).then_inc(written[n % 2], 16)
                        if n < NS or more:
                            load_slot(sp, arrived4, i + 1, s)

                if NIT > 1:
                    with sp.Fori(0, NIT - 1) as it:
                        step(it, True)
                step(NIT - 1, False)
                for b in range(2):
                    sp.wait_ge(written[b], 16 * NS * NIT + W4)

            @block.tensor
            def _(pe):
                def spread(it, n, first=False):
                    pe.wait_ge(arrived4[n % NS], it * 64 + 32 * (n // NS + 1))
                    if not first:
                        pe.wait_ge(u_made4, it * (2 * NN) + 2 * n)
                    broadcast_gate(gate_ps4, n % NS).then_inc(spread4, 1)

                pe.sem_inc(turned4, T4)
                spread(0, 0, True)

                def step(it, more):
                    for n in range(NN):
                        if n + 1 < NN or more:
                            spread(it, n + 1)
                        pe.wait_ge(x2_made, it * (2 * NN) + 2 * (n + 1))
                        for k in range(TG):
                            if k != 3:
                                pe.wait_ge(staged, it * (NN * TG) + n * TG + (k if k > 3 else k + 1))
                            for v in range(2):
                                for j in range(NJ):
                                    block_in = xc[n % 2][:, j, :].rearrange("c (p t) -> c t p", t=NT)[:, 2 * k + v, :]
                                    last = nc.tensor.transpose(
                                        out_ps[k % 4][:, v * C + j * P:v * C + (j + 1) * P], block_in, ident[:, :])
                            last.then_inc(turned4, 1)

                if NIT > 1:
                    with pe.Fori(0, NIT - 1) as it:
                        step(it, True)
                step(NIT - 1, False)

            @block.scalar
            def _(act):
                act.sem_inc(staged, E4)
                for b in range(2):
                    act.sem_inc(written[b], W4)

                def relu(it, n):
                    h = n // NS % 2
                    for j in range(NJ):
                        act.wait_ge(u_made4, it * (2 * NN) + 2 * n + j + 1)
                        u = xc[n % 2][:, j, :]
                        nc.scalar.activation(u, u, ACT.Relu, bias=bn[:, 7, j:j + 1],
                                             scale=curs[:, h, NJ + j:NJ + j + 1]).then_inc(relu_made, 1)

                relu(0, 0)

                def step(it, more):
                    for n in range(NN):
                        if n + 1 < NN or more:
                            relu(it, n + 1)
                        act.wait_ge(written[n % 2], it * (16 * NS) + 16 * (n // 2) + W4)
                        for k in range(TG):
                            act.wait_ge(turned4, it * (NN * TG) + n * TG + k + 1 + T4)
                            nc.scalar.activation(xin[n % 2][:, 2 * k:2 * k + 2, :].rearrange("p t c -> p (t c)"),
                                                 out_ps[k % 4], ACT.Identity).then_inc(staged, 1)

                if NIT > 1:
                    with act.Fori(0, NIT - 1) as it:
                        step(it, True)
                step(NIT - 1, False)

            @block.vector
            def _(dve):
                def make_u(it, n):
                    h, s = n // NS % 2, n % NS
                    if s == 0:
                        nc.vector.tensor_copy(curs[:, h:h + 1, :], par[:, bass.ds(it * 2 + n // NS, 1), :]
                                              ).then_inc(cur_made4, 1)
                        dve.wait_ge(cur_made4, it * 2 + n // NS + 1)
                    dve.wait_ge(spread4, it * NN + n + 1)
                    dve.wait_ge(turned4, it * (NN * TG) + (n - 1) * TG + T4)
                    for j in range(NJ):
                        nc.vector.scalar_tensor_tensor(
                            fours(xc[n % 2][:, j, :]), fours(slots[s][:, j, :]), curs[:, h, j:j + 1],
                            gate_ps4, ALU.add, ALU.mult).then_inc(u_made4, 1)

                make_u(0, 0)

                def step(it, more):
                    for n in range(NN):
                        if n + 1 < NN or more:
                            make_u(it, n + 1)
                        for j in range(NJ):
                            dve.wait_ge(relu_made, it * (2 * NN) + 2 * n + j + 1)
                            u = xc[n % 2][:, j, :]
                            nc.vector.tensor_tensor(u, u, slots[n % NS][:, j, :], ALU.add).then_inc(x2_made, 1)

                if NIT > 1:
                    with dve.Fori(0, NIT - 1) as it:
                        step(it, True)
                step(NIT - 1, False)


def kernel(**inputs):
    import numpy as np
    import concourse.bacc as bacc
    from concourse.bass_utils import run_bass_kernel_spmd

    a = {name: np.asarray(value) for name, value in inputs.items()}
    C = a["x"].shape[3]
    halves = lambda v: v.reshape(C // 128, 128, -1).transpose(1, 0, 2)
    arrays = {
        "x": a["x"],
        "conv_k": halves(a["L0_conv_kernel"].reshape(9, C).T),
        "w1": halves(a["L1_conv_ca_w1"].T),
        "w2": a["L1_conv_ca_w2"].T,
        "lsa": a["L1_conv_lsa_w"].reshape(1, -1),
        "A": a["L1_conv_A"],
        "d_w": a["L1_conv_d_w"],
        "d_b": a["L1_conv_d_b"],
        "B_w": a["L1_conv_B_w"],
        "B_b": a["L1_conv_B_b"],
        "C_w": a["L1_conv_C_w"],
        "C_b": a["L1_conv_C_b"],
        "gamma": halves(a["L1_conv_bn_gamma"])[:, :, 0],
        "beta": halves(a["L1_conv_bn_beta"])[:, :, 0],
    }
    nc = bacc.Bacc("TRN2", target_bir_lowering=False, num_devices=1)
    args = []
    arrays = {f"{name}_dram": np.ascontiguousarray(v) for name, v in arrays.items()}
    for name, v in arrays.items():
        args.append(nc.dram_tensor(name, v.shape, mybir.dt.from_np(v.dtype), kind="ExternalInput").ap())
    out = nc.dram_tensor("out_dram", a["x"].shape, mybir.dt.float32, kind="ExternalOutput").ap()
    binary_conv_then_gated_ssm_block(nc, *args, out)
    return run_bass_kernel_spmd(nc, [arrays], core_ids=[0]).results[0]["out_dram"]
```
